# Optimizing a Trainium2 kernel written in Bass

```python
import numpy as np
import jax
import jax.numpy as jnp

def _softmax(x, axis=-1):
    return jax.nn.softmax(x, axis=axis)

def _gelu(x):
    return jax.nn.gelu(x, approximate=True)

def _silu(x):
    return jax.nn.silu(x)

def _sigmoid(x):
    return jax.nn.sigmoid(x)

def _layernorm(x, axis=-1, eps=1e-05):
    m = jnp.mean(x, axis=axis, keepdims=True)
    v = jnp.var(x, axis=axis, keepdims=True)
    return (x - m) / jnp.sqrt(v + eps)

def _scatter_add(tgt, idx, src, axis=0):
    return tgt.at[idx].add(src)

def _segment_sum(src, seg, n):
    return jax.ops.segment_sum(src, seg, n)
kernel_name = 'mk_gps_d1_gnn_r8_ba4b7d'

def setup_inputs(seed: int=0):
    np.random.seed(seed)
    _w = jnp.asarray

    def _rec_inputs():
        import jax
        import jax.numpy as jnp
        _gk = jax.random.key(seed)
        x = -0.000364 + 1 * jax.random.normal(jax.random.fold_in(_gk, 1), (3750, 512), jnp.float32)
        src = jax.random.randint(jax.random.fold_in(_gk, 2), (60000,), 0, 3750, jnp.int32)
        dst = jnp.minimum((3750 * jax.random.uniform(jax.random.fold_in(_gk, 3), (60000,)) ** 2.0).astype(jnp.int32), 29999)
        _o = jnp.argsort(dst, stable=True)
        src = src[_o]
        dst = dst[_o]
        return (x, src, dst)
    x, src, dst = _rec_inputs()

    def _L0_gnn_setup():
        import jax, jax.numpy as jnp
        import numpy as np
        N = 3750
        E = 60000
        IN = 512
        H1 = 512
        H2 = 128
        NM = 375
        EPS = 1e-05
        key = jax.random.key(seed)
        ks = jax.random.split(key, 20)
        s = 0.05
        return {'x': jax.random.normal(ks[0], (N, IN), dtype=jnp.float32), 'edge_index': jax.random.randint(ks[1], (2, E), 0, N, dtype=jnp.int64), 'mask_idx': jax.random.randint(ks[2], (NM,), 0, N, dtype=jnp.int64), 'enc_mask_token': jnp.zeros((1, IN), dtype=jnp.float32), 'W1': jax.random.normal(ks[3], (IN, H1), dtype=jnp.float32) * s, 'b1': jnp.zeros((H1,), dtype=jnp.float32), 'g1': jnp.ones((H1,), dtype=jnp.float32), 'beta1': jnp.zeros((H1,), dtype=jnp.float32), 'W2': jax.random.normal(ks[4], (H1, H2), dtype=jnp.float32) * s, 'b2': jnp.zeros((H2,), dtype=jnp.float32), 'W_e2d': jax.random.normal(ks[5], (H2, H2), dtype=jnp.float32) * s, 'W3': jax.random.normal(ks[6], (H2, H1), dtype=jnp.float32) * s, 'b3': jnp.zeros((H1,), dtype=jnp.float32), 'g2': jnp.ones((H1,), dtype=jnp.float32), 'beta2': jnp.zeros((H1,), dtype=jnp.float32), 'W4': jax.random.normal(ks[7], (H1, IN), dtype=jnp.float32) * s, 'b4': jnp.zeros((IN,), dtype=jnp.float32)}
    _L0_gnn_all = _L0_gnn_setup()
    _L0_gnn_in = {k: v for k, v in _L0_gnn_all.items() if k in ('mask_idx', 'enc_mask_token', 'W1', 'b1', 'g1', 'beta1', 'W2', 'b2', 'W_e2d', 'W3', 'b3', 'g2', 'beta2', 'W4', 'b4')}
    del _L0_gnn_all

    def _L0_mix_setup():
        import jax, jax.numpy as jnp
        import numpy as np
        HEADS = 8
        EPS_LN = 1e-05
        EPS_NORM = 1e-08
        key = jax.random.key(seed)
        ks = jax.random.split(key, 3)
        B, N, C = (4, 1024, 512)
        x = jax.random.normal(ks[0], (B, N, C), dtype=jnp.float32)
        qkv_w = jax.random.normal(ks[1], (3 * C, C), dtype=jnp.float32) / np.sqrt(C)
        qkv_b = jnp.zeros((3 * C,), dtype=jnp.float32)
        out_w = jax.random.normal(ks[2], (C, C), dtype=jnp.float32) / np.sqrt(C)
        out_b = jnp.zeros((C,), dtype=jnp.float32)
        ln_gamma = jnp.ones((C,), dtype=jnp.float32)
        ln_beta = jnp.zeros((C,), dtype=jnp.float32)
        return {'x': x, 'qkv_w': qkv_w, 'qkv_b': qkv_b, 'out_w': out_w, 'out_b': out_b, 'ln_gamma': ln_gamma, 'ln_beta': ln_beta}
    _L0_mix_all = _L0_mix_setup()
    _L0_mix_in = {k: v for k, v in _L0_mix_all.items() if k in ('qkv_w', 'qkv_b', 'out_w', 'out_b', 'ln_gamma', 'ln_beta')}
    del _L0_mix_all

    def _L0_ffn_setup():
        import jax, jax.numpy as jnp
        import numpy as np
        B, S, D, F, E = (4, 256, 512, 256, 8)
        key = jax.random.key(seed)
        k = jax.random.split(key, 5)
        x = jax.random.normal(k[0], (B, S, D), dtype=jnp.float32)
        Ws = jax.random.normal(k[1], (D, E), dtype=jnp.float32) * 0.02
        bs = jnp.zeros((E,), dtype=jnp.float32)
        W1 = jax.random.normal(k[2], (E, D, F), dtype=jnp.float32) * 0.02
        b1 = jnp.zeros((E, F), dtype=jnp.float32)
        W2 = jax.random.normal(k[3], (E, F, D), dtype=jnp.float32) * 0.02
        b2 = jnp.zeros((E, D), dtype=jnp.float32)
        return {'x': x, 'Ws': Ws, 'bs': bs, 'W1': W1, 'b1': b1, 'W2': W2, 'b2': b2}
    _L0_ffn_all = _L0_ffn_setup()
    _L0_ffn_in = {k: v for k, v in _L0_ffn_all.items() if k in ('Ws', 'bs', 'W1', 'b1', 'W2', 'b2')}
    del _L0_ffn_all
    return {'x': x, 'src': src, 'dst': dst, 'L0_gnn_mask_idx': _L0_gnn_in['mask_idx'], 'L0_gnn_enc_mask_token': _L0_gnn_in['enc_mask_token'], 'L0_gnn_W1': _L0_gnn_in['W1'], 'L0_gnn_b1': _L0_gnn_in['b1'], 'L0_gnn_g1': _L0_gnn_in['g1'], 'L0_gnn_beta1': _L0_gnn_in['beta1'], 'L0_gnn_W2': _L0_gnn_in['W2'], 'L0_gnn_b2': _L0_gnn_in['b2'], 'L0_gnn_W_e2d': _L0_gnn_in['W_e2d'], 'L0_gnn_W3': _L0_gnn_in['W3'], 'L0_gnn_b3': _L0_gnn_in['b3'], 'L0_gnn_g2': _L0_gnn_in['g2'], 'L0_gnn_beta2': _L0_gnn_in['beta2'], 'L0_gnn_W4': _L0_gnn_in['W4'], 'L0_gnn_b4': _L0_gnn_in['b4'], 'L0_mix_qkv_w': _L0_mix_in['qkv_w'], 'L0_mix_qkv_b': _L0_mix_in['qkv_b'], 'L0_mix_out_w': _L0_mix_in['out_w'], 'L0_mix_out_b': _L0_mix_in['out_b'], 'L0_mix_ln_gamma': _L0_mix_in['ln_gamma'], 'L0_mix_ln_beta': _L0_mix_in['ln_beta'], 'L0_ffn_Ws': _L0_ffn_in['Ws'], 'L0_ffn_bs': _L0_ffn_in['bs'], 'L0_ffn_W1': _L0_ffn_in['W1'], 'L0_ffn_b1': _L0_ffn_in['b1'], 'L0_ffn_W2': _L0_ffn_in['W2'], 'L0_ffn_b2': _L0_ffn_in['b2']}

def reference(x, src, dst, L0_gnn_mask_idx, L0_gnn_enc_mask_token, L0_gnn_W1, L0_gnn_b1, L0_gnn_g1, L0_gnn_beta1, L0_gnn_W2, L0_gnn_b2, L0_gnn_W_e2d, L0_gnn_W3, L0_gnn_b3, L0_gnn_g2, L0_gnn_beta2, L0_gnn_W4, L0_gnn_b4, L0_mix_qkv_w, L0_mix_qkv_b, L0_mix_out_w, L0_mix_out_b, L0_mix_ln_gamma, L0_mix_ln_beta, L0_ffn_Ws, L0_ffn_bs, L0_ffn_W1, L0_ffn_b1, L0_ffn_W2, L0_ffn_b2):
    import jax
    import jax.numpy as jnp

    def _L0_gnn_ref(x, edge_index, mask_idx, enc_mask_token, W1, b1, g1, beta1, W2, b2, W_e2d, W3, b3, g2, beta2, W4, b4):
        import jax, jax.numpy as jnp
        import numpy as np
        N = 3750
        E = 60000
        IN = 512
        H1 = 512
        H2 = 128
        NM = 375
        EPS = 1e-05
        src, dst = (edge_index[0], edge_index[1])
        deg = jnp.ones((N,), dtype=x.dtype).at[dst].add(1.0)
        dinv = jax.lax.rsqrt(deg)
        enorm = (dinv[src] * dinv[dst])[:, None]
        snorm = (1.0 / deg)[:, None]

        def prop(h):
            return jax.ops.segment_sum(h[src] * enorm, dst, num_segments=N) + h * snorm

        def gcn(h, W, b):
            return prop(h @ W) + b

        def bn(h, g, b):
            m = h.mean(axis=0)
            v = h.var(axis=0)
            return g * (h - m) * jax.lax.rsqrt(v + EPS) + b
        xm = x.at[mask_idx].set(enc_mask_token[0])
        h = jax.nn.relu(bn(gcn(xm, W1, b1), g1, beta1))
        z = gcn(h, W2, b2)
        rep = z @ W_e2d.T
        rep = rep.at[mask_idx].set(0.0)
        h2 = jax.nn.relu(bn(gcn(rep, W3, b3), g2, beta2))
        recon = gcn(h2, W4, b4)
        return recon

    def _L0_mix_ref(x, qkv_w, qkv_b, out_w, out_b, ln_gamma, ln_beta):
        import jax, jax.numpy as jnp
        import numpy as np
        HEADS = 8
        EPS_LN = 1e-05
        EPS_NORM = 1e-08
        B, N, C = x.shape
        h = HEADS
        d = C // h
        residual = x
        mu = jnp.mean(x, axis=-1, keepdims=True)
        var = jnp.var(x, axis=-1, keepdims=True)
        xn = (x - mu) / jnp.sqrt(var + EPS_LN) * ln_gamma + ln_beta
        qkv = xn @ qkv_w.T + qkv_b
        qkv = qkv.reshape(B, N, 3, h, d).transpose(2, 0, 3, 1, 4)
        q, k, v = (qkv[0], qkv[1], qkv[2])
        q = jax.nn.elu(q) + 1.0
        k = jax.nn.elu(k) + 1.0
        kv = jnp.einsum('bhnd,bhne->bhde', k, v)
        k_sum = jnp.sum(k, axis=2)
        out = jnp.einsum('bhnd,bhde->bhne', q, kv)
        normalizer = jnp.einsum('bhnd,bhd->bhn', q, k_sum)
        out = out / (normalizer[..., None] + EPS_NORM)
        out = out.transpose(0, 2, 1, 3).reshape(B, N, C)
        out = out @ out_w.T + out_b
        return out + residual

    def _L0_ffn_ref(x, Ws, bs, W1, b1, W2, b2):
        import jax, jax.numpy as jnp
        import numpy as np
        B, S, D, F, E = (4, 256, 512, 256, 8)
        Bb, Ss, Dd = x.shape
        xt = x.reshape(-1, Dd)
        logits = xt @ Ws + bs
        probs = jax.nn.softmax(logits, axis=-1)
        prob_max = jnp.max(probs, axis=-1)
        routes = jnp.argmax(probs, axis=-1)
        onehot = jax.nn.one_hot(routes, W1.shape[0], dtype=xt.dtype)

        def expert_ffn(w1, bb1, w2, bb2):
            h = jax.nn.gelu(xt @ w1 + bb1, approximate=False)
            return h @ w2 + bb2
        y = jax.vmap(expert_ffn)(W1, b1, W2, b2)
        out = jnp.einsum('te,etd->td', onehot, y)
        out = out * prob_max[:, None]
        return out.reshape(Bb, Ss, Dd)
    edge_index = jnp.stack([src, dst])
    xn = _layernorm(x, axis=-1)
    x = x + _L0_gnn_ref(xn, edge_index, L0_gnn_mask_idx, L0_gnn_enc_mask_token, L0_gnn_W1, L0_gnn_b1, L0_gnn_g1, L0_gnn_beta1, L0_gnn_W2, L0_gnn_b2, L0_gnn_W_e2d, L0_gnn_W3, L0_gnn_b3, L0_gnn_g2, L0_gnn_beta2, L0_gnn_W4, L0_gnn_b4) + _L0_mix_ref(xn[None], L0_mix_qkv_w, L0_mix_qkv_b, L0_mix_out_w, L0_mix_out_b, L0_mix_ln_gamma, L0_mix_ln_beta)[0]
    x = x + _L0_ffn_ref(_layernorm(x, axis=-1)[None], L0_ffn_Ws, L0_ffn_bs, L0_ffn_W1, L0_ffn_b1, L0_ffn_W2, L0_ffn_b2)[0]
    return x

_drawn_inputs = setup_inputs


def setup_inputs(seed=0):
    import zlib

    import numpy as np

    out = dict(_drawn_inputs(seed))
    spreads = {'L0_gnn_enc_mask_token': (0.0, 0.8),
     'L0_gnn_b1': (0.0, 0.8),
     'L0_gnn_g1': (1.0, 0.2),
     'L0_gnn_beta1': (0.0, 0.347),
     'L0_gnn_b2': (0.0, 0.1),
     'L0_gnn_b3': (0.0, 0.8),
     'L0_gnn_g2': (1.0, 0.2),
     'L0_gnn_beta2': (0.0, 0.1),
     'L0_gnn_b4': (0.0, 0.1),
     'L0_mix_qkv_b': (0.0, 0.1),
     'L0_mix_out_b': (0.0, 0.1),
     'L0_mix_ln_gamma': (1.0, 0.6),
     'L0_mix_ln_beta': (0.0, 0.1),
     'L0_ffn_bs': (0.0, 0.8),
     'L0_ffn_b1': (0.0, 0.8),
     'L0_ffn_b2': (0.0, 0.712)}
    factors = {'L0_ffn_Ws': 4.139, 'L0_ffn_W1': 6.416, 'L0_ffn_W2': 5.998}
    for name, (base, spread) in spreads.items():
        noise = np.random.default_rng([zlib.crc32(name.encode()), seed]).standard_normal(out[name].shape)
        drawn = base * np.exp(spread * noise) if base else spread * noise
        out[name] = jnp.asarray(drawn.astype(out[name].dtype))
    for name, factor in factors.items():
        out[name] = (out[name] * factor).astype(out[name].dtype)
    return out
```

```python
import concourse.bass as bass
from concourse import mybir
from contextlib import ExitStack

F32 = mybir.dt.float32
I32 = mybir.dt.int32
BF16 = mybir.dt.bfloat16
F16 = mybir.dt.float16
ALU = mybir.AluOpType
ACT = mybir.ActivationFunctionType
AX = mybir.AxisListType

P = 128
N = 3750
NT = (N + P - 1) // P
NP = NT * P
D = 512
C = D // P
HID = 128
E = 60000
NM = 375
MP = 125
MC = NM // MP
HD = 64
XE = 8
FF = 256
FC = FF // P
EPS = 1e-5
EPS_NORM = 1e-8
LN_BOUND = 22.7

SUB = 32
NSUB = NP // SUB
KB = NT * SUB
NB = (E + P - 1) // P
EROWS = E // P
ETAIL = E - EROWS * P
BC = 4
GRP = 2
STG = 8
SW = STG * SUB
NSTRIP = NSUB // STG
CREDIT = 2
RND = 6
NR = NT // RND
RW = RND * P
NG = 8
GW = NP // NG
Q3 = 3

COLS = {}
for _name, _w in (("mix_gamma", C), ("mix_beta", C), ("b1", C), ("g1", C), ("beta1", C), ("b2", 1),
                  ("b3", C), ("g2", C), ("beta2", C), ("ffn_b1", XE * FC)):
    COLS[_name] = (sum(w for _, w in COLS.values()), _w)
NCOLS = sum(w for _, w in COLS.values())
ROWS = {}
for _name, _w in (("qkv_b", 3 * D), ("out_b", D), ("b4", D), ("ffn_bs", XE)):
    ROWS[_name] = (sum(w for _, w in ROWS.values()), _w)
NROWS = sum(w for _, w in ROWS.values())


class Order:

    def __init__(self, eng, sem):
        self.eng, self.sem, self.base, self.k = eng, sem, 0, 0

    def then(self, ins):
        ins.then_inc(self.sem, 1)
        self.k += 1
        self.eng.wait_ge(self.sem, self.base + self.k)

    def enter(self, i, per_turn):
        self.saved = (self.base, self.k, per_turn)
        self.base, self.k = self.base + self.k + i * per_turn, 0

    def leave(self, turns):
        assert self.k == self.saved[2], (self.k, self.saved[2])
        self.base, self.k = self.saved[0], self.saved[1] + turns * self.saved[2]


class Memory:

    def __init__(self, nc, ctx, tag):
        self.nc, self.ctx, self.tag, self.taken = nc, ctx, tag, []

    def sb(self, name, shape, dt=F32):
        return self.ctx.enter_context(self.nc.sbuf_tensor(f"{self.tag}_{name}", shape, dt))

    def bank(self, name, dt=F32, banks=1):
        return self.ctx.enter_context(self.nc.psum_tensor(f"{self.tag}_{name}_ps", [P, 512 * banks], dt))

    def sem(self, name):
        self.taken.append(self.nc.alloc_semaphore(f"{self.tag}_{name}"))
        return self.taken[-1]

    def end_phase(self):
        self.nc.clear_and_free_semaphores(self.taken)
        self.nc.all_engine_barrier()

    def sems(self, name, n):
        return [self.sem(f"{name}{i}") for i in range(n)]


class Kept:

    def __init__(self, m):
        self.ident = m.sb("ident", [P, P])
        self.ident16 = m.sb("ident16", [P, P], F16)
        self.ones_row = m.sb("ones_row", [1, P])
        self.zero16 = m.sb("zero16", [P, P], F16)
        self.zero32 = m.sb("zero32", [P, P])
        self.nhalf = m.sb("nhalf", [P, 1])
        self.cols = m.sb("cols", [P, NCOLS])
        self.rows = m.sb("rows", [1, NROWS])
        self.masked = m.sb("masked", [P, NT])
        self.kept = m.sb("kept", [P, NT])
        self.valid = m.sb("valid", [P, NT])
        self.dinv = m.sb("dinv", [P, NT])
        self.dinv_b = m.sb("dinv_b", [P, NP])
        self.h_scale = m.sb("h_scale", [P, 2])
        self.dsc = m.sb("dsc", [P, 2, NT])

    def col(self, name, j=0, w=1):
        o = COLS[name][0]
        return self.cols[:, o + j:o + j + w]

    def row(self, name, a=0, b=None):
        o, w = ROWS[name]
        return self.rows[:, o + a:o + (w if b is None else b)]


def power_of_two_scale(v, order, k, bound, tmp_i, tmp_f):
    order.then(v.tensor_scalar(tmp_f[:, 0:1], bound, 1e-30, 1e30, ALU.max, ALU.min))
    order.then(v.tensor_scalar(tmp_i[:, 0:1], tmp_f[:, 0:1].bitcast(I32), 23, None,
                               ALU.arith_shift_right))
    v.tensor_scalar(tmp_i[:, 1:2], tmp_i[:, 0:1], -1.0, 268.0, ALU.mult, ALU.add)
    order.then(v.tensor_scalar(tmp_i[:, 2:3], tmp_i[:, 0:1], 14.0, None, ALU.subtract))
    order.then(v.tensor_scalar(k.h_scale[:, :].bitcast(I32), tmp_i[:, 1:3], 23, None,
                               ALU.arith_shift_left))
    v.tensor_scalar(k.dsc[:, 0, :], k.dinv[:, :], k.h_scale[:, 0:1], None, ALU.mult)
    order.then(v.tensor_scalar(k.dsc[:, 1, :], k.dinv[:, :], k.h_scale[:, 1:2], None, ALU.mult))


def build_graph(nc, k, src, dst, mask_idx, token, cols, rows, graph_d):
    with ExitStack() as ctx:
        m = Memory(nc, ctx, "build")
        raw = m.sb("raw", [P, 2, BC, P], I32)
        parts_i = m.sb("parts_i", [P, 4, BC, P], I32)
        parts = m.sb("parts", [P, 4, BC, P])
        span = m.sb("span", [P, 3, BC, P])
        first_last = m.sb("first_last", [P, 2, BC])
        key = m.sb("key", [P, BC * P])
        src_lo = m.sb("src_lo", [P, BC * P])
        tri = m.sb("tri", [P, P])
        iota_pass = m.sb("iota_pass", [P, P])
        iota_block = m.sb("iota_block", [P, BC])
        pass_base = m.sb("pass_base", [P, P])
        counts = m.sb("counts", [P, 8])
        counts_i = m.sb("counts_i", [P, 1], I32)
        table = m.sb("table", [1, 2, P], I32)
        mraw = m.sb("mraw", [MP, MC], I32)
        mpart_i = m.sb("mpart_i", [MP, 2, MC], I32)
        mpart = m.sb("mpart", [MP, 2, MC])
        mhot = m.sb("mhot", [MP, 2, MC, P])
        iota16 = m.sb("iota16", [P, KB], F16)
        hot_col = m.sb("hot_col", [P, GRP, KB], F16)
        hot_src = m.sb("hot_src", [P, GRP, P], F16)
        ones16 = m.sb("ones16", [P, P], F16)
        strip = [m.sb(f"strip{u}", [P, NT, SW], F16) for u in range(2)]
        deg = m.sb("deg", [P, NP])
        degn = m.sb("degn", [P, NT])
        ones32 = m.sb("ones32", [P, P])
        diag = m.sb("diag", [P, NT, P])
        tok = m.sb("tok", [P, D])
        tmp_i = m.sb("tmp_i", [P, 4], I32)
        tmp_f = m.sb("tmp_f", [P, 4])
        acc = [m.bank(f"acc{u}", banks=2) for u in range(2)]
        turn = [m.bank(f"turn{u}") for u in range(3)]
        deg_ps = m.bank("deg_ps")

        edges_in, params_in = m.sem("edges_in"), m.sem("params_in")
        pads_set, fills, consts = m.sem("pads_set"), m.sem("fills"), m.sem("consts")
        v_order, a_order = m.sem("v_order"), m.sem("a_order")
        keys_ready, keys_turned = m.sem("keys_ready"), m.sem("keys_turned")
        spans_ready, spans_turned = m.sem("spans_ready"), m.sem("spans_turned")
        counts_ready, table_sum, table_ready = m.sem("counts_ready"), m.sem("table_sum"), m.sem("table_ready")
        mask_ready, mask_sum = m.sem("mask_ready"), m.sem("mask_sum")
        hot_ready, hot_used = m.sem("hot_ready"), m.sem("hot_used")
        pass_sum, pass_copied = m.sem("pass_sum"), m.sem("pass_copied")
        deg_sum, deg_copied = m.sem("deg_sum"), m.sem("deg_copied")
        strip_out = m.sems("strip_out", 2)
        degn_ready, pow_ready, diag_ready = m.sem("degn_ready"), m.sem("pow_ready"), m.sem("diag_ready")
        dinvb_sum, dinvb_copied = m.sem("dinvb_sum"), m.sem("dinvb_copied")

        with nc.Block() as block:

            def store_strip(sp, s, u):
                sp.wait_ge(pass_copied, CREDIT + STG * s + STG)
                sp.dma_start(graph_d[:, :, bass.ds(s * SW, SW)].rearrange("k p d -> p k d"),
                             strip[u][:, :, :]).then_inc(strip_out[u], 16)

            def build_strip(pe, s, u):
                for w in range(STG):
                    build_pass(pe, s, w)
                pe.wait_ge(pass_copied, CREDIT + STG * s + STG)
                pe.wait_ge(deg_copied, s)
                for kt in range(NT):
                    last = pe.matmul(deg_ps[:, 0:SW], ones16[:, :], strip[u][:, kt, :],
                                     start=(kt == 0), stop=(kt == NT - 1))
                last.then_inc(deg_sum, 1)

            def build_pass(pe, s, w):
                t = s * STG + w
                a = acc[w % 2]
                g0 = pe.value_load(table[0:1, 0, bass.ds(t, 1)], min_val=0, max_val=1 << 20)
                g1 = pe.value_load(table[0:1, 0, bass.ds(t + 1, 1)], min_val=0, max_val=1 << 20)
                pe.wait_ge(pass_copied, t + 1)
                for h in range(2):
                    pe.matmul(a[:, 512 * h:512 * h + 2], k.zero16[:, :], k.zero16[:, 0:2],
                              start=True, stop=False, skip_group_check=True)
                pe.matmul(a[:, bass.ds((s * (SW // P) + w * SUB // P) * SUB, SUB)], k.ident16[:, :],
                          k.ident16[:, w * SUB % P:w * SUB % P + SUB],
                          start=False, stop=False, skip_group_check=True)
                with pe.Fori(g0, g1) as g:
                    for j in range(GRP):
                        pe.wait_ge(hot_ready, GRP * g + j + 1)
                        pe.matmul(a[:, 0:512], hot_src[:, j, :], hot_col[:, j, 0:512],
                                  start=False, stop=False, skip_group_check=True)
                        pe.matmul(a[:, 512:KB], hot_src[:, j, :], hot_col[:, j, 512:KB], start=False,
                                  stop=False, skip_group_check=True).then_inc(hot_used, 1)
                for h in range(2):
                    last = pe.matmul(a[:, 512 * h:512 * h + 2], k.zero16[:, :], k.zero16[:, 0:2],
                                     start=False, stop=True, skip_group_check=True)
                last.then_inc(pass_sum, 1)

            def copy_strip(a, s, u, stored):
                a.wait_ge(strip_out[u], stored)
                for w in range(STG):
                    a.wait_ge(pass_sum, s * STG + w + 1)
                    a.activation(strip[u][:, :, w * SUB:(w + 1) * SUB],
                                 acc[w % 2][:, 0:KB].rearrange("p (k d) -> p k d", d=SUB),
                                 ACT.Copy).then_inc(pass_copied, 1)
                a.wait_ge(deg_sum, s + 1)
                a.activation(deg[:, bass.ds(s * SW, SW)], deg_ps[:, 0:SW], ACT.Copy).then_inc(deg_copied, 1)

            @block.sync
            def _(sp):
                sp.wait_ge(pads_set, 2)
                for i, a in enumerate((src, dst)):
                    for j in range(BC):
                        r = min(P, EROWS - j * P)
                        sp.dma_start(raw[0:r, i, j, :], a[j * P * P:(j * P + r) * P]
                                     .rearrange("(r p) -> r p", p=P)).then_inc(edges_in, 16)
                    r = EROWS - (BC - 1) * P
                    sp.dma_start(raw[r:r + 1, i, BC - 1, 0:ETAIL], a[EROWS * P:E]
                                 .rearrange("(r p) -> r p", r=1)).then_inc(edges_in, 16)
                sp.dma_start(mraw[:, :], mask_idx).then_inc(params_in, 16)
                sp.dma_start(tok[:, :], token).then_inc(params_in, 16)
                sp.dma_start(k.cols[:, :], cols).then_inc(params_in, 16)
                sp.dma_start(k.rows[:, :], rows).then_inc(params_in, 16)
                with sp.Fori(0, NSTRIP - 2, 2) as i:
                    for u in range(2):
                        store_strip(sp, i + u, u)
                store_strip(sp, NSTRIP - 1, 0)
                sp.wait_ge(params_in, 64)
                sp.wait_ge(strip_out[0], 16 * 8)
                sp.wait_ge(strip_out[1], 16 * 7)

            @block.gpsimd
            def _(g):
                g.memset(raw[:, 0, :, :], 0).then_inc(pads_set, 1)
                g.memset(raw[:, 1, :, :], NP + 2 * SUB).then_inc(pads_set, 1)
                g.memset(k.ident[:, :], 1.0).then_inc(fills, 1)
                g.memset(k.ident16[:, :], 1.0).then_inc(fills, 1)
                g.memset(tri[:, :], 1.0).then_inc(fills, 1)
                g.memset(k.valid[:, :], 1.0).then_inc(fills, 1)
                g.memset(k.ones_row[:, :], 1.0).then_inc(fills, 1)
                g.memset(k.zero16[:, :], 0.0).then_inc(fills, 1)
                g.memset(k.zero32[:, :], 0.0).then_inc(fills, 1)
                g.memset(k.nhalf[:, :], -0.5).then_inc(fills, 1)
                g.memset(ones16[:, :], 1.0).then_inc(fills, 1)
                g.memset(ones32[:, :], 1.0).then_inc(fills, 1)
                g.wait_ge(fills, 10)
                for t in (k.ident, k.ident16):
                    g.affine_select(out=t[:, :], in_=t[:, :], compare_op=ALU.is_equal, fill=0.0, base=0,
                                    pattern=[[-1, P]], channel_multiplier=1).then_inc(consts, 1)
                g.affine_select(out=tri[:, :], in_=tri[:, :], compare_op=ALU.is_gt, fill=0.0, base=0,
                                pattern=[[1, P]], channel_multiplier=-1).then_inc(consts, 1)
                g.affine_select(out=k.valid[:, :], in_=k.valid[:, :], compare_op=ALU.is_gt, fill=0.0,
                                base=N, pattern=[[-P, NT]], channel_multiplier=-1).then_inc(consts, 1)
                for t, pat, base, cm in ((iota16[:, :], [[1, KB]], 0, 0), (pass_base[:, :], [[KB, P]], 0, 0),
                                         (iota_pass[:, :], [[1, P]], 0, 0), (iota_block[:, :], [[P, BC]], 1, 1)):
                    g.iota(t, pat, base=base, channel_multiplier=cm,
                           allow_small_or_imprecise_dtypes=True).then_inc(consts, 1)
                g.wait_ge(degn_ready, 1)
                g.tensor_tensor(k.dinv[:, :], degn[:, :], k.nhalf[:, 0:1].to_broadcast([P, NT]),
                                ALU.pow).then_inc(pow_ready, 1)

            @block.vector
            def _(v):
                o = Order(v, v_order)
                v.wait_ge(edges_in, 16 * 10)
                v.tensor_scalar(parts_i[:, 0], raw[:, 0], P - 1, None, ALU.bitwise_and)
                v.tensor_scalar(parts_i[:, 1], raw[:, 0], 7, None, ALU.arith_shift_right)
                v.tensor_scalar(parts_i[:, 2], raw[:, 1], SUB - 1, None, ALU.bitwise_and)
                o.then(v.tensor_scalar(parts_i[:, 3], raw[:, 1], 5, None, ALU.arith_shift_right))
                v.tensor_copy(parts[:, 0], parts_i[:, 0])
                o.then(v.tensor_copy(parts[:, 1], parts_i[:, 3]))
                o.then(v.tensor_scalar(parts[:, 2], parts_i[:, 1], float(SUB), None, ALU.mult))
                o.then(v.scalar_tensor_tensor(parts[:, 3], parts[:, 1], float(KB), parts[:, 2],
                                              ALU.mult, ALU.add))
                v.tensor_tensor(parts[:, 3], parts[:, 3], parts_i[:, 2], ALU.add).then_inc(keys_ready, 1)
                v.wait_ge(keys_turned, 1)
                v.tensor_copy(src_lo[:, :], turn[0][:, :])
                o.then(v.tensor_copy(key[:, :], turn[1][:, :]))
                v.tensor_reduce(first_last[:, 0, :], parts[:, 1], AX.X, ALU.min)
                o.then(v.tensor_reduce(first_last[:, 1, :], parts[:, 1], AX.X, ALU.max))
                v.wait_ge(consts, 8)
                for j in range(BC):
                    v.tensor_scalar(span[:, 0, j, :], iota_pass[:, :], first_last[:, 0, j:j + 1], None, ALU.is_ge)
                    o.then(v.tensor_scalar(span[:, 1, j, :], iota_pass[:, :], first_last[:, 1, j:j + 1], None, ALU.is_le))
                    o.then(v.tensor_tensor(span[:, 2, j, :], span[:, 0, j, :], span[:, 1, j, :], ALU.mult))
                    v.tensor_scalar(span[:, 0, j, :], span[:, 2, j, :], iota_block[:, j:j + 1], None, ALU.mult)
                    o.then(v.tensor_scalar(span[:, 1, j, :], span[:, 2, j, :], 513.0, None, ALU.mult))
                    o.then(v.tensor_tensor(span[:, 1, j, :], span[:, 1, j, :], span[:, 0, j, :], ALU.subtract))
                v.sem_inc(spans_ready, 1)
                v.wait_ge(spans_turned, 1)
                v.tensor_reduce(counts[:, 0:1], turn[0][:, :], AX.X, ALU.max)
                o.then(v.tensor_reduce(counts[:, 1:2], turn[1][:, :], AX.X, ALU.max))
                o.then(v.tensor_scalar(counts[:, 2:3], counts[:, 1:2], -1.0, 512.0, ALU.mult, ALU.add))
                o.then(v.tensor_tensor(counts[:, 3:4], counts[:, 0:1], counts[:, 2:3], ALU.subtract))
                o.then(v.tensor_scalar(counts[:, 3:4], counts[:, 3:4], 1.0, float(GRP - 1), ALU.max, ALU.add))
                o.then(v.tensor_scalar(counts[:, 4:5], counts[:, 3:4], 1.0 / GRP, -0.5 + 0.5 / GRP, ALU.mult, ALU.add))
                o.then(v.tensor_copy(counts_i[:, :], counts[:, 4:5]))
                v.tensor_copy(counts[:, 5:6], counts_i[:, :])
                v.tensor_scalar(counts[:, 6:7], counts[:, 2:3], float(NB - 1), None, ALU.min)
                o.then(v.tensor_scalar(counts[:, 7:8], counts_i[:, :], -float(GRP), None, ALU.mult))
                v.sem_inc(counts_ready, 1)
                v.wait_ge(table_sum, 1)
                v.tensor_copy(table[:, 0, :], turn[2][0:1, 0:P])
                v.tensor_copy(table[:, 1, :], turn[2][0:1, P:2 * P]).then_inc(table_ready, 1)
                v.wait_ge(params_in, 64)
                v.tensor_scalar(mpart_i[:, 0, :], mraw[:, :], P - 1, None, ALU.bitwise_and)
                o.then(v.tensor_scalar(mpart_i[:, 1, :], mraw[:, :], 7, None, ALU.arith_shift_right))
                o.then(v.tensor_copy(mpart[:, :, :], mpart_i[:, :, :]))
                for c in range(MC):
                    v.tensor_scalar(mhot[:, 0, c, :], iota_pass[0:MP, :], mpart[:, 0, c:c + 1], None, ALU.is_equal)
                    last = v.tensor_scalar(mhot[:, 1, c, :], iota_pass[0:MP, :], mpart[:, 1, c:c + 1], None, ALU.is_equal)
                last.then_inc(mask_ready, 1)
                v.wait_ge(mask_sum, 1)
                o.then(v.tensor_scalar(k.masked[:, :], turn[2][:, 0:NT], 1.0, None, ALU.min))
                v.tensor_scalar(k.kept[:, :], k.masked[:, :], -1.0, 1.0, ALU.mult, ALU.add)
                v.wait_ge(table_ready, 1)
                with v.Fori(0, NSUB) as t:
                    g0 = v.value_load(table[0:1, 0, bass.ds(t, 1)], min_val=0, max_val=1 << 20)
                    g1 = v.value_load(table[0:1, 0, bass.ds(t + 1, 1)], min_val=0, max_val=1 << 20)
                    off = v.value_load(table[0:1, 1, bass.ds(t, 1)])
                    with v.Fori(g0, g1) as g:
                        for j in range(GRP):
                            v.wait_ge(hot_used, GRP * g + j + 1)
                            b = off + GRP * g + j
                            v.tensor_scalar(hot_src[:, j, :], iota16[:, 0:P], src_lo[:, bass.ds(b, 1)],
                                            None, ALU.is_equal)
                            v.tensor_scalar(hot_col[:, j, :], iota16[:, :], pass_base[:, bass.ds(t, 1)],
                                            key[:, bass.ds(b, 1)], ALU.add, ALU.is_equal).then_inc(hot_ready, 1)
                v.wait_ge(deg_copied, NSTRIP)
                ident_t = k.ident[:, :].rearrange("p (a d) -> p a d", a=1).to_broadcast([P, NT, P])
                o.then(v.tensor_tensor(diag[:, :, :], deg[:, :].rearrange("p (t d) -> p t d", d=P),
                                       ident_t, ALU.mult))
                v.tensor_reduce(degn[:, :], diag[:, :, :], AX.X, ALU.add).then_inc(degn_ready, 1)
                v.wait_ge(pow_ready, 1)
                v.tensor_tensor(diag[:, :, :], ident_t,
                                k.dinv[:, :].rearrange("p (t a) -> p t a", a=1).to_broadcast([P, NT, P]),
                                ALU.mult).then_inc(diag_ready, 1)
                for h in range(NG):
                    v.wait_ge(dinvb_sum, h + 1)
                    v.tensor_copy(k.dinv_b[:, h * GW:(h + 1) * GW],
                                  acc[h % 2][:, 0:GW]).then_inc(dinvb_copied, 1)
                o.then(v.tensor_reduce(tmp_f[:, 1:2], tok[:, :], AX.X, ALU.max, apply_absolute_value=True))
                o.then(v.tensor_scalar(tmp_f[:, 1:2], tmp_f[:, 1:2], LN_BOUND, None, ALU.max))
                power_of_two_scale(v, o, k, tmp_f[:, 1:2], tmp_i, tmp_f)

            @block.tensor
            def _(pe):
                pe.wait_ge(consts, 8)
                pe.wait_ge(keys_ready, 1)
                for j in range(BC):
                    pe.transpose(turn[0][:, j * P:(j + 1) * P], parts[:, 0, j, :], k.ident[:, :])
                    last = pe.transpose(turn[1][:, j * P:(j + 1) * P], parts[:, 3, j, :], k.ident[:, :])
                last.then_inc(keys_turned, 1)
                pe.wait_ge(spans_ready, 1)
                for j in range(BC):
                    pe.transpose(turn[0][:, j * P:(j + 1) * P], span[:, 0, j, :], k.ident[:, :])
                    last = pe.transpose(turn[1][:, j * P:(j + 1) * P], span[:, 1, j, :], k.ident[:, :])
                last.then_inc(spans_turned, 1)
                pe.wait_ge(counts_ready, 1)
                pe.matmul(turn[2][0:1, 0:P], counts[:, 5:6], tri[:, :], start=True, stop=True)
                pe.matmul(turn[2][0:1, P:2 * P], counts[:, 6:7], k.ident[:, :], start=True, stop=False)
                pe.matmul(turn[2][0:1, P:2 * P], counts[:, 7:8], tri[:, :], start=False,
                          stop=True).then_inc(table_sum, 1)
                pe.wait_ge(mask_ready, 1)
                for c in range(MC):
                    last = pe.matmul(turn[2][:, 0:NT], mhot[:, 0, c, :], mhot[:, 1, c, 0:NT],
                                     start=(c == 0), stop=(c == MC - 1))
                last.then_inc(mask_sum, 1)
                pe.wait_ge(table_ready, 1)
                pe.sem_inc(hot_used, GRP)
                with pe.Fori(0, NSTRIP - 2, 2) as s:
                    for u in range(2):
                        build_strip(pe, s + u, u)
                build_strip(pe, NSTRIP - 1, 0)
                pe.wait_ge(diag_ready, 1)
                for h in range(NG):
                    if h >= 2:
                        pe.wait_ge(dinvb_copied, h - 1)
                    pe.matmul(acc[h % 2][:, 0:GW], ones32[:, :],
                              diag[:, :, :].rearrange("p t d -> p (t d)")[:, h * GW:(h + 1) * GW],
                              start=True, stop=True).then_inc(dinvb_sum, 1)

            @block.scalar
            def _(a):
                a.sem_inc(pass_copied, CREDIT)
                with a.Fori(0, NSTRIP - 2, 2) as s:
                    for u in range(2):
                        copy_strip(a, s + u, u, 8 * s)
                copy_strip(a, NSTRIP - 1, 0, 8 * (NSTRIP - 1))
        m.end_phase()


def norm_and_qkv(nc, k, x, token, wqkvT, H, qT, kvs, res_d):
    with ExitStack() as ctx:
        m = Memory(nc, ctx, "qkv")
        w = m.sb("w", [P, C, 3 * D])
        tok = m.sb("tok", [P, D])
        xin = [m.sb(f"xin{u}", [P, D]) for u in range(2)]
        xn = [m.sb(f"xn{u}", [P, D]) for u in range(2)]
        res = [m.sb(f"res{u}", [P, D]) for u in range(2)]
        xm = m.sb("xm", [P, D])
        xmT = m.sb("xmT", [P, C, P])
        expq, relq = m.sb("expq", [P, D]), m.sb("relq", [P, D])
        expk, relk = m.sb("expk", [P, D]), m.sb("relk", [P, D])
        kf, vf = m.sb("kf", [P, D]), m.sb("vf", [P, D])
        tm = m.sb("tm", [P, D])
        st = m.sb("st", [P, 2, 6])
        ag = m.sb("ag", [P, 2, 2])
        ve = m.sb("ve", [P, 2])
        rstd = m.sb("rstd", [P, 2])
        turn, q_ps, k_ps, v_ps = m.bank("turn"), m.bank("q"), m.bank("k"), m.bank("v")
        kv_ps, ks_ps = m.bank("kv"), m.bank("ks")

        w_in, v_order, v_steps = m.sem("w_in"), m.sem("v_order"), m.sem("v_steps")
        x_in, x_used = m.sems("x_in", 2), m.sem("x_used")
        var_ready, rstd_ready = m.sem("var_ready"), m.sem("rstd_ready")
        xm_ready, turned, xmT_ready = m.sem("xm_ready"), m.sem("turned"), m.sem("xmT_ready")
        qkv_sum, exp_ready, v_ready = m.sem("qkv_sum"), m.sem("exp_ready"), m.sem("v_ready")
        qk_ready, kv_sum = m.sem("qk_ready"), m.sem("kv_sum")
        tm_ready, tm_used = m.sem("tm_ready"), m.sem("tm_used")
        res_ready, res_out = m.sem("res_ready"), m.sems("res_out", 2)
        kvs_ready = m.sem("kvs_ready")

        with nc.Block() as block:

            @block.sync
            def _(sp):
                sp.dma_start(w[:, :, :], wqkvT.rearrange("(c p) n -> p c n", p=P)).then_inc(w_in, 16)
                sp.dma_start(tok[:, :], token).then_inc(w_in, 16)
                for u in range(2):
                    sp.dma_start(xin[u][:, :], x[u * P:(u + 1) * P, :]).then_inc(x_in[u], 16)
                with sp.Fori(0, NT // 2 - 1) as i:
                    for u in range(2):
                        sp.wait_ge(x_used, 2 * i + u + 1)
                        sp.dma_start(xin[u][:, :], x[bass.ds((2 * i + 2 + u) * P, P), :]).then_inc(x_in[u], 16)
                for u in range(2):
                    sp.wait_ge(res_out[u], 16 * (NT // 2))

            @block.gpsimd
            def _(g):
                with g.Fori(0, NT // 2) as i:
                    for u in range(2):
                        t = 2 * i + u
                        for j in range(2):
                            g.wait_ge(var_ready, 2 * t + j + 1)
                            g.tensor_tensor(rstd[:, j:j + 1], ve[:, j:j + 1], k.nhalf[:, :],
                                            ALU.pow).then_inc(rstd_ready, 1)

            @block.vector
            def _(v):
                o = Order(v, v_order)

                def norm(t, u, j, source, target):
                    o.then(v.bn_stats(st[:, j, :], source))
                    v.sem_inc(v_steps)
                    o.then(v.bn_aggr(ag[:, j, :], st[:, j, :]))
                    v.tensor_scalar(ve[:, j:j + 1], ag[:, j, 1:2], EPS, None, ALU.add).then_inc(var_ready, 1)
                    v.wait_ge(rstd_ready, 2 * t + j + 1)
                    return v.tensor_scalar(target, source, ag[:, j, 0:1], rstd[:, j:j + 1], ALU.subtract, ALU.mult)

                with v.Fori(0, NT // 2) as i:
                    o.enter(i, 2 * 11)
                    for u in range(2):
                        t = 2 * i + u
                        v.wait_ge(x_in[u], 16 * i + 16)
                        v.wait_ge(res_out[u], 16 * i)
                        o.then(norm(t, u, 0, xin[u][:, :], xn[u][:, :]))
                        v.tensor_tensor(res[u][:, :], xin[u][:, :], xn[u][:, :], ALU.add).then_inc(x_used, 1)
                        v.wait_ge(turned, t)
                        norm(t, u, 1, xn[u][:, :], xm[:, :]).then_inc(xm_ready, 1)
                        o.then(v.tensor_scalar(tm[:, :], tok[:, :], k.masked[:, bass.ds(t, 1)], None, ALU.mult))
                        o.then(v.scalar_tensor_tensor(tm[:, :], xn[u][:, :], k.kept[:, bass.ds(t, 1)],
                                                      tm[:, :], ALU.mult, ALU.add))
                        o.then(v.tensor_scalar(tm[:, :], tm[:, :], k.dsc[:, 0, bass.ds(t, 1)], None, ALU.mult))
                        o.then(v.tensor_copy(H[:, bass.ds(t, 1), 0, :], tm[:, :]))
                        o.then(v.tensor_tensor(H[:, bass.ds(t, 1), 1, :], tm[:, :], H[:, bass.ds(t, 1), 0, :], ALU.subtract))
                        v.wait_ge(exp_ready, 2 * t + 2)
                        v.tensor_scalar(relq[:, :], q_ps[:, :], 0.0, None, ALU.max)
                        o.then(v.tensor_scalar(relk[:, :], k_ps[:, :], 0.0, None, ALU.max))
                        v.wait_ge(kv_sum, t)
                        v.scalar_tensor_tensor(qT[:, :, bass.ds(t * P, P)], expq[:, :].rearrange("p (c n) -> p c n", c=C), 1.0,
                                               relq[:, :].rearrange("p (c n) -> p c n", c=C), ALU.min, ALU.add)
                        v.scalar_tensor_tensor(kf[:, :], expk[:, :], 1.0, relk[:, :], ALU.min,
                                               ALU.add).then_inc(qk_ready, 1)
                        v.wait_ge(qk_ready, t + 1)
                    o.leave(NT // 2)
                v.wait_ge(kv_sum, NT)
                v.tensor_copy(kvs[:, 0:D], kv_ps[:, :])
                v.tensor_copy(kvs[:, D:D + C], ks_ps[:, 0:C]).then_inc(kvs_ready, 1)

            @block.scalar
            def _(a):
                with a.Fori(0, NT // 2) as i:
                    for u in range(2):
                        t = 2 * i + u
                        a.wait_ge(x_used, t + 1)
                        a.dma_start(res_d[bass.ds(t * P, P), :], res[u][:, :]).then_inc(res_out[u], 16)
                        a.wait_ge(turned, t + 1)
                        for c in range(C):
                            last = a.activation(xmT[:, c, :], turn[:, c * P:(c + 1) * P], ACT.Identity,
                                                bias=k.col("mix_beta", c), scale=k.col("mix_gamma", c))
                        last.then_inc(xmT_ready, 1)
                        a.wait_ge(qkv_sum, t + 1)
                        a.wait_ge(qk_ready, t)
                        a.activation(expq[:, :], q_ps[:, :], ACT.Exp).then_inc(exp_ready, 1)
                        a.activation(expk[:, :], k_ps[:, :], ACT.Exp).then_inc(exp_ready, 1)
                        a.wait_ge(kv_sum, t)
                        a.activation(vf[:, :], v_ps[:, :], ACT.Copy, scale=k.valid[:, bass.ds(t, 1)]).then_inc(v_ready, 1)

            @block.tensor
            def _(pe):
                pe.wait_ge(w_in, 32)
                for b in (kv_ps, ks_ps):
                    pe.matmul(b[:, 0:2], k.zero32[:, :], k.zero32[:, 0:2], start=True, stop=False, skip_group_check=True)
                with pe.Fori(0, NT // 2) as i:
                    for u in range(2):
                        t = 2 * i + u
                        pe.wait_ge(xm_ready, t + 1)
                        pe.wait_ge(xmT_ready, t)
                        for c in range(C):
                            last = pe.transpose(turn[:, c * P:(c + 1) * P], xm[:, c * P:(c + 1) * P], k.ident[:, :])
                        last.then_inc(turned, 1)
                        pe.wait_ge(xmT_ready, t + 1)
                        pe.wait_ge(qk_ready, t)
                        for j in range(C):
                            for c in range(C):
                                pe.matmul(q_ps[:, j * P:(j + 1) * P], w[:, c, j * P:(j + 1) * P], xmT[:, c, :],
                                          start=(c == 0), stop=False)
                            pe.matmul(q_ps[:, j * P:(j + 1) * P], k.row("qkv_b", j * P, (j + 1) * P),
                                      k.ones_row[:, :], start=False, stop=True)
                        pe.wait_ge(v_ready, t)
                        for n, b in ((1, k_ps), (2, v_ps)):
                            for c in range(C):
                                pe.matmul(b[:, :], xmT[:, c, :], w[:, c, n * D:(n + 1) * D], start=(c == 0), stop=False)
                            last = pe.matmul(b[:, :], k.ones_row[:, :], k.row("qkv_b", n * D, (n + 1) * D),
                                             start=False, stop=True)
                        last.then_inc(qkv_sum, 1)
                        pe.wait_ge(qk_ready, t + 1)
                        pe.wait_ge(v_ready, t + 1)
                        for c in range(C):
                            pe.matmul(kv_ps[:, c * P:(c + 1) * P], kf[:, c * P:(c + 1) * P], vf[:, c * P:(c + 1) * P],
                                      start=False, stop=False, skip_group_check=True)
                            last = pe.matmul(ks_ps[:, c:c + 1], kf[:, c * P:(c + 1) * P], k.valid[:, bass.ds(t, 1)],
                                             start=False, stop=False, skip_group_check=True)
                        last.then_inc(kv_sum, 1)
        m.end_phase()


def attention_out(nc, k, woT, qT, kvs, res_d, mix_d):
    W = 2 * P
    with ExitStack() as ctx:
        m = Memory(nc, ctx, "att")
        wo = m.sb("wo", [P, C, D])
        kvbd = m.sb("kvbd", [P, C, P])
        ksel = m.sb("ksel", [P, C, XE])
        hsel = m.sb("hsel", [8, C, P])
        onesh = m.sb("onesh", [8, C * P])
        rn = m.sb("rn", [8, W])
        den = m.sb("den", [8, W])
        rnb = m.sb("rnb", [P, C, W])
        oT = m.sb("oT", [P, C, W])
        res = [m.sb(f"res{u}", [P, D]) for u in range(2)]
        mix = [m.sb(f"mix{u}", [P, D]) for u in range(2)]
        o_ps, r_ps = m.bank("o", banks=2), m.bank("r", banks=2)
        n_ps = m.bank("n")
        y_ps = [m.bank(f"y{u}") for u in range(2)]

        w_in, sel_ready, v_order = m.sem("w_in"), m.sem("sel_ready"), m.sem("v_order")
        fills, hsel_ready = m.sem("fills"), m.sem("hsel_ready")
        o_sum, r_sum, rn_ready, rnb_ready, oT_ready = (m.sem(n_) for n_ in ("o_sum", "r_sum", "rn_ready", "rnb_ready", "oT_ready"))
        y_sum, y_read = m.sem("y_sum"), m.sem("y_read")
        res_in, mix_out = m.sems("res_in", 2), m.sems("mix_out", 2)

        with nc.Block() as block:

            @block.sync
            def _(sp):
                sp.dma_start(wo[:, :, :], woT.rearrange("(c p) n -> p c n", p=P)).then_inc(w_in, 16)
                with sp.Fori(0, NT // 2) as i:
                    for u in range(2):
                        sp.wait_ge(y_read, 2 * i)
                        sp.dma_start(res[u][:, :], res_d[bass.ds((2 * i + u) * P, P), :]).then_inc(res_in[u], 16)
                for u in range(2):
                    sp.wait_ge(mix_out[u], 16 * (NT // 2))

            @block.gpsimd
            def _(g):
                g.memset(kvbd[:, :, :], 0.0).then_inc(fills, 1)
                g.memset(ksel[:, :, :], 0.0).then_inc(fills, 1)
                g.memset(onesh[:, :], 1.0).then_inc(fills, 1)
                g.wait_ge(fills, 3)
                g.affine_select(out=onesh[:, :], in_=onesh[:, :], compare_op=ALU.is_ge, fill=0.0, base=0,
                                pattern=[[1, C * P]], channel_multiplier=-HD).then_inc(fills, 1)
                g.wait_ge(fills, 4)
                g.affine_select(out=hsel[:, :, :].rearrange("h c p -> h (c p)"), in_=onesh[:, :], compare_op=ALU.is_gt, fill=0.0,
                                base=HD, pattern=[[-1, C * P]], channel_multiplier=HD).then_inc(hsel_ready, 1)

            @block.vector
            def _(v):
                v.wait_ge(fills, 3)
                for c in range(C):
                    for h in range(2):
                        r = slice(h * HD, (h + 1) * HD)
                        v.tensor_copy(kvbd[r, c, r], kvs[r, c * P + h * HD:c * P + (h + 1) * HD])
                        last = v.tensor_copy(ksel[r, c, 2 * c + h:2 * c + h + 1], kvs[r, D + c:D + c + 1])
                last.then_inc(sel_ready, 1)
                o = Order(v, v_order)
                with v.Fori(0, NT // 2) as i:
                    o.enter(i, 1)
                    v.wait_ge(o_sum, i + 1)
                    o.then(v.tensor_scalar(den[:, :], n_ps[0:8, 0:W], EPS_NORM, None, ALU.add))
                    v.reciprocal(rn[:, :], den[:, :]).then_inc(rn_ready, 1)
                    v.wait_ge(rnb_ready, i + 1)
                    v.tensor_tensor(oT[:, :, :], o_ps[:, :].rearrange("p (c n) -> p c n", c=C), rnb[:, :, :],
                                    ALU.mult).then_inc(oT_ready, 1)
                    for u in range(2):
                        v.wait_ge(y_sum, 2 * i + u + 1)
                        v.wait_ge(res_in[u], 16 * i + 16)
                        v.wait_ge(mix_out[u], 16 * i)
                        v.tensor_tensor(mix[u][:, :], y_ps[u][:, :], res[u][:, :], ALU.add).then_inc(y_read, 1)
                    o.leave(NT // 2)

            @block.scalar
            def _(a):
                with a.Fori(0, NT // 2) as i:
                    a.wait_ge(r_sum, i + 1)
                    a.wait_ge(oT_ready, i)
                    a.activation(rnb[:, :, :], r_ps[:, :].rearrange("p (c n) -> p c n", c=C), ACT.Copy).then_inc(rnb_ready, 1)
                    for u in range(2):
                        a.wait_ge(y_read, 2 * i + u + 1)
                        a.dma_start(mix_d[bass.ds((2 * i + u) * P, P), :], mix[u][:, :]).then_inc(mix_out[u], 16)

            @block.tensor
            def _(pe):
                pe.wait_ge(w_in, 16)
                pe.wait_ge(sel_ready, 1)
                pe.wait_ge(hsel_ready, 1)
                with pe.Fori(0, NT // 2) as i:
                    pe.wait_ge(oT_ready, i)
                    pe.wait_ge(rn_ready, i)
                    for c in range(C):
                        pe.matmul(n_ps[0:8, 0:W], ksel[:, c, :], qT[:, c, bass.ds(i * W, W)], start=(c == 0), stop=(c == C - 1))
                    for c in range(C):
                        last = pe.matmul(o_ps[:, c * W:(c + 1) * W], kvbd[:, c, :], qT[:, c, bass.ds(i * W, W)],
                                         start=True, stop=True)
                    last.then_inc(o_sum, 1)
                    pe.wait_ge(rn_ready, i + 1)
                    pe.wait_ge(rnb_ready, i)
                    for c in range(C):
                        last = pe.matmul(r_ps[:, c * W:(c + 1) * W], hsel[:, c, :], rn[:, :], start=True, stop=True)
                    last.then_inc(r_sum, 1)
                    pe.wait_ge(oT_ready, i + 1)
                    for u in range(2):
                        pe.wait_ge(y_read, 2 * i)
                        for c in range(C):
                            pe.matmul(y_ps[u][:, :], oT[:, c, u * P:(u + 1) * P], wo[:, c, :], start=(c == 0), stop=False)
                        pe.matmul(y_ps[u][:, :], k.ones_row[:, :], k.row("out_b"), start=False, stop=False)
                        pe.matmul(y_ps[u][:, :], k.ones_row[:, :], k.row("b4"), start=False, stop=True).then_inc(y_sum, 1)
        m.end_phase()


RING = 6


def load_strips(sp, graph_d, ring, ring_in, ring_used, rounds_before):
    with sp.Fori(0, NR) as r:
        with sp.Fori(0, NT // RING) as i:
            for u in range(RING):
                n = r * NT + i * RING + u
                sp.wait_ge(ring_used, n + 1)
                sp.dma_start(ring[u][:, :], graph_d[bass.ds(i * RING + u, 1), :, bass.ds(r * RW, RW)]
                             .rearrange("k p d -> (k p) d")).then_inc(ring_in[u], 16)


def sum_strips(pe, k, r, H, ring, ring_in, ring_used, acc):
    for j in range(RND):
        pe.matmul(acc[j][:, 0:2], k.zero16[:, :], k.zero16[:, 0:2], start=True, stop=False, skip_group_check=True)
    with pe.Fori(0, NT // RING) as i:
        for u in range(RING):
            pe.wait_ge(ring_in[u], 16 * (r * (NT // RING) + i + 1))
            for j in range(RND):
                for h in range(2):
                    last = pe.matmul(acc[j][:, :], ring[u][:, j * P:(j + 1) * P],
                                     H[:, bass.ds(i * RING + u, 1), h, :], start=False, stop=False,
                                     skip_group_check=True)
            last.then_inc(ring_used, 1)
    for j in range(RND):
        last = pe.matmul(acc[j][:, 0:2], k.zero16[:, :], k.zero16[:, 0:2], start=False, stop=True, skip_group_check=True)
    return last


def first_convolution(nc, k, graph_d, H, w1, uT):
    with ExitStack() as ctx:
        m = Memory(nc, ctx, "conv1")
        ring = [m.sb(f"ring{u}", [P, RW], F16) for u in range(RING)]
        w = m.sb("w", [P, C, D])
        pn = [m.sb(f"pn{u}", [P, D]) for u in range(2)]
        pT = [m.sb(f"pT{u}", [P, C, P]) for u in range(2)]
        acc = [m.bank(f"acc{j}") for j in range(RND)]
        turn, u_ps = m.bank("turn"), m.bank("u")
        w_in, ring_in, ring_used = m.sem("w_in"), m.sems("ring_in", RING), m.sem("ring_used")
        round_sum, pn_ready, turned, pT_ready = m.sem("round_sum"), m.sem("pn_ready"), m.sem("turned"), m.sem("pT_ready")
        u_sum, u_ready = m.sem("u_sum"), m.sem("u_ready")

        with nc.Block() as block:

            @block.sync
            def _(sp):
                sp.dma_start(w[:, :, :], w1.rearrange("(c p) n -> p c n", p=P)).then_inc(w_in, 16)
                load_strips(sp, graph_d, ring, ring_in, ring_used, 0)

            @block.vector
            def _(v):
                with v.Fori(0, NR) as r:
                    v.wait_ge(round_sum, r + 1)
                    for j in range(RND + 1):
                        if j < RND:
                            v.wait_ge(turned, RND * r + j - 1 if j else RND * r)
                            v.tensor_scalar(pn[j % 2][:, :], acc[j][:, :], k.dsc[:, 1, bass.ds(r * RND + j, 1)], None,
                                            ALU.mult).then_inc(pn_ready, 1)
                        if j:
                            n = r * RND + j - 1
                            v.wait_ge(u_sum, n + 1)
                            for c in range(C):
                                last = v.tensor_scalar(uT[:, c, bass.ds(n * P, P)], u_ps[:, c * P:(c + 1) * P],
                                                       k.col("b1", c), None, ALU.add)
                            last.then_inc(u_ready, 1)

            @block.scalar
            def _(a):
                with a.Fori(0, NT // 2) as i:
                    for u in range(2):
                        a.wait_ge(turned, 2 * i + u + 1)
                        a.wait_ge(u_sum, 2 * i)
                        a.activation(pT[u][:, :, :], turn[:, :].rearrange("p (c n) -> p c n", c=C), ACT.Copy).then_inc(pT_ready, 1)

            @block.tensor
            def _(pe):
                pe.wait_ge(w_in, 16)
                pe.sem_inc(ring_used, RING)
                with pe.Fori(0, NR) as r:
                    pe.wait_ge(pn_ready, r * RND)
                    sum_strips(pe, k, r, H, ring, ring_in, ring_used, acc).then_inc(round_sum, 1)
                    for j in range(RND):
                        n = r * RND + j
                        pe.wait_ge(pn_ready, n + 1)
                        pe.wait_ge(pT_ready, n)
                        for c in range(C):
                            last = pe.transpose(turn[:, c * P:(c + 1) * P], pn[j % 2][:, c * P:(c + 1) * P], k.ident[:, :])
                        last.then_inc(turned, 1)
                        pe.wait_ge(pT_ready, n + 1)
                        pe.wait_ge(u_ready, n)
                        for f in range(C):
                            for c in range(C):
                                last = pe.matmul(u_ps[:, f * P:(f + 1) * P], w[:, c, f * P:(f + 1) * P],
                                                 pT[j % 2][:, c, :], start=(c == 0), stop=(c == C - 1))
                        last.then_inc(u_sum, 1)
        m.end_phase()


def batch_norm_relu(nc, k, uT, gamma, beta, tag):
    with ExitStack() as ctx:
        m = Memory(nc, ctx, tag)
        st = m.sb("st", [P, C, NG, 6])
        ag = m.sb("ag", [P, C, 2])
        ve, rs, sc, sh = (m.sb(n_, [P, C]) for n_ in ("ve", "rs", "sc", "sh"))
        v_order, var_ready, rstd_ready, coef_ready, done = (m.sem(n_) for n_ in ("v_order", "var_ready", "rstd_ready", "coef_ready", "done"))
        with nc.Block() as block:

            @block.vector
            def _(v):
                o = Order(v, v_order)
                for c in range(C):
                    for g in range(NG):
                        last = v.bn_stats(st[:, c, g, :], uT[:, c, g * GW:min((g + 1) * GW, N)])
                    o.then(last)
                    o.then(v.bn_aggr(ag[:, c, :], st[:, c, :, :].rearrange("p g s -> p (g s)")))
                v.tensor_scalar(ve[:, :], ag[:, :, 1], EPS, None, ALU.add).then_inc(var_ready, 1)
                v.wait_ge(rstd_ready, 1)
                o.then(v.tensor_tensor(sc[:, :], rs[:, :], k.col(gamma, 0, C), ALU.mult))
                o.then(v.tensor_tensor(sh[:, :], sc[:, :], ag[:, :, 0], ALU.mult))
                v.tensor_tensor(sh[:, :], k.col(beta, 0, C), sh[:, :], ALU.subtract).then_inc(coef_ready, 1)
                v.wait_ge(coef_ready, 1)
                for c in range(2):
                    o.then(v.tensor_scalar(uT[:, c, :], uT[:, c, :], sc[:, c:c + 1], sh[:, c:c + 1], ALU.mult, ALU.add))
                    last = v.tensor_scalar(uT[:, c, :], uT[:, c, :], 0.0, None, ALU.max)
                o.then(last)

            @block.gpsimd
            def _(g):
                g.wait_ge(var_ready, 1)
                g.tensor_tensor(rs[:, :], ve[:, :], k.nhalf[:, 0:1].to_broadcast([P, C]), ALU.pow).then_inc(rstd_ready, 1)

            @block.scalar
            def _(a):
                a.wait_ge(coef_ready, 1)
                for c in range(2, C):
                    a.activation(uT[:, c, :], uT[:, c, :], ACT.Relu, scale=sc[:, c:c + 1], bias=sh[:, c:c + 1]).then_inc(done, 1)
                a.wait_ge(done, 2)
        m.end_phase()


def narrow_features(nc, k, source, chunks, weight, HQ, factor, tag):
    with ExitStack() as ctx:
        m = Memory(nc, ctx, tag)
        w = m.sb("w", [P, chunks, HID])
        fac = m.sb("fac", [P, NT])
        q = [m.sb(f"q{u}", [P, Q3, HID]) for u in range(2)]
        q_ps = [m.bank(f"q{u}") for u in range(2)]
        w_in, q_sum, q_read, v_order = m.sem("w_in"), m.sem("q_sum"), m.sem("q_read"), m.sem("v_order")
        with nc.Block() as block:

            @block.sync
            def _(sp):
                sp.dma_start(w[:, :, :], weight.rearrange("(c p) n -> p c n", p=P)).then_inc(w_in, 16)

            @block.vector
            def _(v):
                o = Order(v, v_order)
                if factor is None:
                    o.then(v.tensor_copy(fac[:, :], k.dinv[:, :]))
                else:
                    o.then(v.tensor_tensor(fac[:, :], k.dinv[:, :], factor[:, :], ALU.mult))
                with v.Fori(0, NT // Q3 // 2) as i:
                    o.enter(i, 2 * 5)
                    for u in range(2):
                        s = 2 * i + u
                        v.wait_ge(q_sum, s + 1)
                        parts = HQ[:, bass.ds(s * Q3, Q3), :, :]
                        v.tensor_tensor(q[u][:, :, :], q_ps[u][:, 0:Q3 * HID].rearrange("p (t n) -> p t n", t=Q3),
                                        fac[:, bass.ds(s * Q3, Q3)].rearrange("p (t a) -> p t a", a=1).to_broadcast([P, Q3, HID]),
                                        ALU.mult).then_inc(q_read, 1)
                        v.wait_ge(q_read, s + 1)
                        o.then(v.tensor_copy(parts[:, :, 0, :], q[u][:, :, :]))
                        o.then(v.tensor_tensor(q[u][:, :, :], q[u][:, :, :], parts[:, :, 0, :], ALU.subtract))
                        o.then(v.tensor_copy(parts[:, :, 1, :], q[u][:, :, :]))
                        o.then(v.tensor_tensor(q[u][:, :, :], q[u][:, :, :], parts[:, :, 1, :], ALU.subtract))
                        o.then(v.tensor_copy(parts[:, :, 2, :], q[u][:, :, :]))
                    o.leave(NT // Q3 // 2)

            @block.tensor
            def _(pe):
                pe.wait_ge(w_in, 16)
                for s in range(NT // Q3):
                    if s >= 2:
                        pe.wait_ge(q_read, s - 1)
                    for t in range(s * Q3, (s + 1) * Q3):
                        for c in range(chunks):
                            last = pe.matmul(q_ps[s % 2][:, t % Q3 * HID:(t % Q3 + 1) * HID],
                                             source[:, c, t * P:(t + 1) * P], w[:, c, :],
                                             start=(c == 0), stop=(c == chunks - 1))
                    last.then_inc(q_sum, 1)
        m.end_phase()


NRING = 5


def narrow_propagation(nc, k, graph_d, HQ, zT, bias, tag):
    with ExitStack() as ctx:
        m = Memory(nc, ctx, tag)
        ring = [m.sb(f"ring{u}", [P, NP], F16) for u in range(NRING)]
        acc = [m.bank(f"acc{g}") for g in range(NG)]
        ring_in, ring_used, z_sum, z_ready, done = m.sems("ring_in", NRING), m.sem("ring_used"), m.sem("z_sum"), m.sem("z_ready"), m.sem("done")
        with nc.Block() as block:

            @block.sync
            def _(sp):
                with sp.Fori(0, NT // NRING) as i:
                    for u in range(NRING):
                        sp.wait_ge(ring_used, i * NRING + u + 1)
                        sp.dma_start(ring[u][:, :], graph_d[bass.ds(i * NRING + u, 1), :, :]
                                     .rearrange("k p d -> (k p) d")).then_inc(ring_in[u], 16)

            @block.tensor
            def _(pe):
                pe.sem_inc(ring_used, NRING)
                for g in range(NG):
                    pe.matmul(acc[g][:, 0:2], k.zero16[:, :], k.zero16[:, 0:2], start=True, stop=False, skip_group_check=True)
                with pe.Fori(0, NT // NRING) as i:
                    for u in range(NRING):
                        pe.wait_ge(ring_in[u], 16 * i + 16)
                        for h in range(3):
                            for g in range(NG):
                                last = pe.matmul(acc[g][:, 0:GW], HQ[:, bass.ds(i * NRING + u, 1), h, :], ring[u][:, g * GW:(g + 1) * GW],
                                                 start=False, stop=False, skip_group_check=True)
                        last.then_inc(ring_used, 1)
                for g in range(NG):
                    last = pe.matmul(acc[g][:, 0:2], k.zero16[:, :], k.zero16[:, 0:2], start=False, stop=True, skip_group_check=True)
                last.then_inc(z_sum, 1)

            @block.vector
            def _(v):
                v.wait_ge(z_sum, 1)
                for g in range(NG):
                    c = slice(g * GW, (g + 1) * GW)
                    v.tensor_tensor(zT[:, 0, c], acc[g][:, 0:GW], k.dinv_b[:, c], ALU.mult).then_inc(z_ready, 1)
                v.wait_ge(z_ready, NG)

            @block.scalar
            def _(a):
                if bias is not None:
                    for g in range(NG):
                        c = slice(g * GW, (g + 1) * GW)
                        a.wait_ge(z_ready, g + 1)
                        a.activation(zT[:, 0, c], zT[:, 0, c], ACT.Identity, bias=k.col(bias)).then_inc(done, 1)
                    a.wait_ge(done, NG)
        m.end_phase()


def widen(nc, k, rT, w3, uT):
    with ExitStack() as ctx:
        m = Memory(nc, ctx, "widen")
        w = m.sb("w", [P, D])
        ps = [m.bank(f"u{j}") for j in range(4)]
        w_in, u_sum, u_read = m.sem("w_in"), m.sem("u_sum"), m.sem("u_read")
        with nc.Block() as block:

            @block.sync
            def _(sp):
                sp.dma_start(w[:, :], w3).then_inc(w_in, 16)

            @block.tensor
            def _(pe):
                pe.wait_ge(w_in, 16)
                for n in range(C * NG):
                    c, g = divmod(n, NG)
                    if n >= 4:
                        pe.wait_ge(u_read, n - 3)
                    pe.matmul(ps[n % 4][:, 0:GW], w[:, c * P:(c + 1) * P], rT[:, 0, g * GW:(g + 1) * GW], start=True, stop=True).then_inc(u_sum, 1)

            @block.scalar
            def _(a):
                for n in range(C * NG):
                    c, g = divmod(n, NG)
                    a.wait_ge(u_sum, n + 1)
                    a.activation(uT[:, c, g * GW:(g + 1) * GW], ps[n % 4][:, 0:GW], ACT.Identity, bias=k.col("b3", c)).then_inc(u_read, 1)
                a.wait_ge(u_read, C * NG)
        m.end_phase()


def last_features(nc, k, hT, w4, G):
    with ExitStack() as ctx:
        m = Memory(nc, ctx, "feat4")
        w = m.sb("w", [P, C, D])
        top = m.sb("top", [P, NT])
        topm = m.sb("topm", [P, 4])
        tmp_i, tmp_f = m.sb("tmp_i", [P, 4], I32), m.sb("tmp_f", [P, 4])
        hf = [m.sb(f"hf{u}", [P, D]) for u in range(2)]
        g_ps = [m.bank(f"g{u}") for u in range(2)]
        t_ps = m.bank("t")
        w_in, g_sum, g_read, top_ready, top_turned, tops_ready, top_sum, v_order = (m.sem(n_) for n_ in (
            "w_in", "g_sum", "g_read", "top_ready", "top_turned", "tops_ready", "top_sum", "v_order"))
        done, hf_ready, lo_ready = m.sem("done"), m.sem("hf_ready"), m.sem("lo_ready")
        Gf = G[:, :, :, :].bitcast(F32)
        topT = m.sb("topT", [1, P])
        with nc.Block() as block:

            @block.sync
            def _(sp):
                sp.dma_start(w[:, :, :], w4.rearrange("(c p) n -> p c n", p=P)).then_inc(w_in, 16)

            @block.tensor
            def _(pe):
                pe.wait_ge(w_in, 16)
                for t in range(NT):
                    if t >= 2:
                        pe.wait_ge(g_read, t - 1)
                    for c in range(C):
                        last = pe.matmul(g_ps[t % 2][:, :], hT[:, c, t * P:(t + 1) * P], w[:, c, :], start=(c == 0), stop=(c == C - 1))
                    last.then_inc(g_sum, 1)
                pe.wait_ge(top_ready, 1)
                pe.transpose(t_ps[0:1, 0:P], topm[:, 0:1], k.ident[:, :]).then_inc(top_turned, 1)
                pe.wait_ge(tops_ready, 1)
                pe.matmul(t_ps[:, 256:257], k.ones_row[:, :], topm[0:1, 1:2], start=True, stop=True).then_inc(top_sum, 1)

            @block.vector
            def _(v):
                o = Order(v, v_order)
                with v.Fori(0, NT // 2) as i:
                    for u in range(2):
                        t = 2 * i + u
                        v.wait_ge(g_sum, t + 1)
                        g = Gf[:, bass.ds(t, 1), :, :].rearrange("p t h n -> p (t h n)")
                        v.tensor_scalar(g, g_ps[u][:, :], k.dinv[:, bass.ds(t, 1)], None, ALU.mult).then_inc(g_read, 1)
                        v.wait_ge(g_read, t + 1)
                        v.tensor_reduce(top[:, bass.ds(t, 1)], g, AX.X, ALU.max, apply_absolute_value=True)
                o.then(v.tensor_copy(hf[0][:, 0:1], w[:, 0, 0:1]))
                v.tensor_reduce(topm[:, 0:1], top[:, :], AX.X, ALU.max).then_inc(top_ready, 1)
                v.wait_ge(top_turned, 1)
                v.tensor_reduce(topm[0:1, 1:2], t_ps[0:1, 0:P], AX.X, ALU.max).then_inc(tops_ready, 1)
                v.wait_ge(top_sum, 1)
                power_of_two_scale(v, o, k, t_ps[:, 256:257], tmp_i, tmp_f)
                with v.Fori(0, NT // 2) as i:
                    o.enter(i, 2)
                    for u in range(2):
                        t = 2 * i + u
                        g = Gf[:, bass.ds(t, 1), :, :].rearrange("p t h n -> p (t h n)")
                        o.then(v.tensor_scalar(hf[u][:, :], g, k.h_scale[:, 0:1], None, ALU.mult))
                        v.tensor_copy(G[:, bass.ds(t, 1), 0, :], hf[u][:, :]).then_inc(hf_ready, 1)
                        v.wait_ge(hf_ready, t + 1)
                        v.tensor_tensor(G[:, bass.ds(t, 1), 1, :], hf[u][:, :], G[:, bass.ds(t, 1), 0, :], ALU.subtract).then_inc(lo_ready, 1)
                    o.leave(NT // 2)
                v.wait_ge(lo_ready, NT)
        m.end_phase()


def last_convolution(nc, k, graph_d, H, mix_d, x2):
    with ExitStack() as ctx:
        m = Memory(nc, ctx, "conv4")
        ring = [m.sb(f"ring{u}", [P, RW], F16) for u in range(RING)]
        mix = [m.sb(f"mix{u}", [P, D]) for u in range(2)]
        acc = [m.bank(f"acc{j}") for j in range(RND)]
        ring_in, ring_used = m.sems("ring_in", RING), m.sem("ring_used")
        mix_in, round_sum, x2_ready = m.sems("mix_in", 2), m.sem("round_sum"), m.sem("x2_ready")
        with nc.Block() as block:

            @block.sync
            def _(sp):
                load_strips(sp, graph_d, ring, ring_in, ring_used, 0)

            @block.scalar
            def _(a):
                with a.Fori(0, NT // 2) as i:
                    for u in range(2):
                        a.wait_ge(x2_ready, 2 * i)
                        a.dma_start(mix[u][:, :], mix_d[bass.ds((2 * i + u) * P, P), :]).then_inc(mix_in[u], 16)

            @block.vector
            def _(v):
                with v.Fori(0, NR) as r:
                    v.wait_ge(round_sum, r + 1)
                    for j in range(RND):
                        n = r * RND + j
                        v.wait_ge(mix_in[j % 2], 16 * (r * (RND // 2) + j // 2 + 1))
                        v.scalar_tensor_tensor(x2[:, bass.ds(n, 1), :], acc[j][:, :], k.dsc[:, 1, bass.ds(n, 1)],
                                               mix[j % 2][:, :], ALU.mult, ALU.add).then_inc(x2_ready, 1)
                v.wait_ge(x2_ready, NT)

            @block.tensor
            def _(pe):
                pe.sem_inc(ring_used, RING)
                with pe.Fori(0, NR) as r:
                    pe.wait_ge(x2_ready, r * RND)
                    sum_strips(pe, k, r, H, ring, ring_in, ring_used, acc).then_inc(round_sum, 1)
        m.end_phase()


def experts(nc, k, x2, ws, w1, w2, b2, out):
    W = 2 * P
    with ExitStack() as ctx:
        m = Memory(nc, ctx, "moe")
        w1s = m.sb("w1", [P, C, XE * FF])
        w2s = m.sb("w2", [P, XE * FC, D])
        wss = m.sb("ws", [P, C, XE])
        b2s = m.sb("b2", [XE, D])
        rank = m.sb("rank", [P, XE])
        xt = [m.sb(f"xt{u}", [P, D]) for u in range(2)]
        xtT = m.sb("xtT", [P, C, W])
        hT = [m.sb(f"hT{u}", [P, FC, W]) for u in range(2)]
        y = [m.sb(f"y{u}", [P, D]) for u in range(2)]
        st, ag, ve, rs = m.sb("st", [P, 6]), m.sb("ag", [P, 2, 2]), m.sb("ve", [P, 2]), m.sb("rs", [P, 2])
        lg = m.sb("lg", [P, 2, 4, XE])
        one = m.sb("one", [P, 2, 8])
        coT = m.sb("coT", [XE, W])
        turn, misc = m.bank("turn"), m.bank("misc")
        h_ps, y_ps = [m.bank(f"h{u}") for u in range(2)], [m.bank(f"y{u}") for u in range(4)]
        w_in, rank_ready, v_order, v_steps = m.sem("w_in"), m.sem("rank_ready"), m.sem("v_order"), m.sem("v_steps")
        var_ready, rstd_ready, xt_ready, turned, xtT_ready = (m.sem(n_) for n_ in ("var_ready", "rstd_ready", "xt_ready", "turned", "xtT_ready"))
        logits, nmax_ready, exp_ready, coef_ready, coef_turned, coT_ready = (m.sem(n_) for n_ in (
            "logits", "nmax_ready", "exp_ready", "coef_ready", "coef_turned", "coT_ready"))
        h_sum, h_ready, y_sum, y_read, out_done = m.sem("h_sum"), m.sem("h_ready"), m.sem("y_sum"), m.sem("y_read"), m.sems("out_done", 2)
        with nc.Block() as block:

            @block.sync
            def _(sp):
                sp.dma_start(wss[:, :, :], ws.rearrange("(c p) n -> p c n", p=P)).then_inc(w_in, 16)
                sp.dma_start(b2s[:, :], b2).then_inc(w_in, 16)
                sp.dma_start(w1s[:, :, :], w1.rearrange("(c p) n -> p c n", p=P)).then_inc(w_in, 16)
                sp.dma_start(w2s[:, :, :], w2.rearrange("(c p) n -> p c n", p=P)).then_inc(w_in, 16)
                with sp.Fori(0, NT // 2) as i:
                    for u in range(2):
                        sp.wait_ge(y_read, (i + 1) * (2 * XE + 2))
                        sp.dma_start(out[bass.ds((2 * i + u) * P, P), :], y[u][:, :]).then_inc(out_done[u], 16)
                for u in range(2):
                    sp.wait_ge(out_done[u], 16 * (NT // 2))

            @block.gpsimd
            def _(g):
                g.iota(rank[:, :], [[-1, XE]], base=XE, channel_multiplier=0,
                       allow_small_or_imprecise_dtypes=True).then_inc(rank_ready, 1)
                with g.Fori(0, NT // 2) as i:
                    for u in range(2):
                        g.wait_ge(var_ready, 2 * i + u + 1)
                        g.tensor_tensor(rs[:, u:u + 1], ve[:, u:u + 1], k.nhalf[:, :], ALU.pow).then_inc(rstd_ready, 1)

            @block.vector
            def _(v):
                o = Order(v, v_order)
                v.wait_ge(rank_ready, 1)
                with v.Fori(0, NT // 2) as i:
                    o.enter(i, 2 * 8)
                    for u in range(2):
                        t = 2 * i + u
                        x = x2[:, bass.ds(t, 1), :].rearrange("p t n -> p (t n)")
                        o.then(v.bn_stats(st[:, :], x))
                        v.sem_inc(v_steps)
                        o.then(v.bn_aggr(ag[:, u, :], st[:, :]))
                        v.tensor_scalar(ve[:, u:u + 1], ag[:, u, 1:2], EPS, None, ALU.add).then_inc(var_ready, 1)
                        v.wait_ge(rstd_ready, t + 1)
                        v.wait_ge(turned, 2 * i)
                        v.tensor_scalar(xt[u][:, :], x, ag[:, u, 0:1], rs[:, u:u + 1], ALU.subtract,
                                        ALU.mult).then_inc(xt_ready, 1)
                        v.wait_ge(logits, t + 1)
                        o.then(v.tensor_reduce(one[:, u, 0:1], misc[:, u * 64:u * 64 + XE], AX.X, ALU.max))
                        o.then(v.tensor_scalar(one[:, u, 1:2], one[:, u, 0:1], -1.0, None, ALU.mult))
                        v.scalar_tensor_tensor(lg[:, u, 1, :], misc[:, u * 64:u * 64 + XE], one[:, u, 0:1], rank[:, :],
                                               ALU.is_ge, ALU.mult).then_inc(nmax_ready, 1)
                        v.wait_ge(exp_ready, t + 1)
                        o.then(v.reciprocal(one[:, u, 3:4], one[:, u, 2:3]))
                        o.then(v.tensor_reduce(one[:, u, 4:5], lg[:, u, 1, :], AX.X, ALU.max))
                        o.then(v.tensor_scalar(lg[:, u, 2, :], lg[:, u, 1, :], one[:, u, 4:5], None, ALU.is_equal))
                        o.then(v.tensor_scalar(lg[:, u, 3, :], lg[:, u, 2, :], one[:, u, 3:4], None, ALU.mult))
                        v.sem_inc(coef_ready, 1)
                    v.wait_ge(coef_turned, i + 1)
                    v.tensor_copy(coT[:, :], misc[0:XE, 128:128 + W]).then_inc(coT_ready, 1)
                    for e in range(XE + 1):
                        for u in range(2):
                            n = i * (2 * XE + 2) + 2 * e + u
                            v.wait_ge(y_sum, n + 1)
                            if e:
                                v.wait_ge(y_read, n - 1)
                                v.scalar_tensor_tensor(y[u][:, :], y_ps[(2 * e + u) % 4][:, :], lg[:, u, 3, e - 1:e], y[u][:, :],
                                                       ALU.mult, ALU.add).then_inc(y_read, 1)
                            else:
                                v.wait_ge(out_done[u], 16 * i)
                                v.tensor_tensor(y[u][:, :], y_ps[(2 * e + u) % 4][:, :],
                                                x2[:, bass.ds(2 * i + u, 1), :].rearrange("p t n -> p (t n)"), ALU.add).then_inc(y_read, 1)
                    o.leave(NT // 2)

            @block.scalar
            def _(a):
                with a.Fori(0, NT // 2) as i:
                    for u in range(2):
                        t = 2 * i + u
                        a.wait_ge(turned, t + 1)
                        if u == 0:
                            a.wait_ge(h_sum, i * XE)
                        a.activation(xtT[:, :, u * P:(u + 1) * P], turn[:, :].rearrange("p (c n) -> p c n", c=C), ACT.Copy).then_inc(xtT_ready, 1)
                        a.wait_ge(nmax_ready, t + 1)
                        a.activation(lg[:, u, 0, :], misc[:, u * 64:u * 64 + XE], ACT.Exp, bias=one[:, u, 1:2],
                                     accum_out=one[:, u, 2:3]).then_inc(exp_ready, 1)
                    for e in range(XE):
                        n = i * XE + e
                        a.wait_ge(h_sum, n + 1)
                        a.wait_ge(y_sum, i * (2 * XE + 2) + 2 * e)
                        for f in range(FC):
                            last = a.activation(hT[e % 2][:, f, :], h_ps[e % 2][:, f * W:(f + 1) * W], ACT.Gelu,
                                                bias=k.col("ffn_b1", e * FC + f))
                        last.then_inc(h_ready, 1)

            @block.tensor
            def _(pe):
                pe.wait_ge(w_in, 64)
                with pe.Fori(0, NT // 2) as i:
                    for u in range(2):
                        t = 2 * i + u
                        pe.wait_ge(xt_ready, t + 1)
                        pe.wait_ge(xtT_ready, t)
                        for c in range(C):
                            last = pe.transpose(turn[:, c * P:(c + 1) * P], xt[u][:, c * P:(c + 1) * P], k.ident[:, :])
                        last.then_inc(turned, 1)
                        pe.wait_ge(xtT_ready, t + 1)
                        for c in range(C):
                            pe.matmul(misc[:, u * 64:u * 64 + XE], xtT[:, c, u * P:(u + 1) * P], wss[:, c, :], start=(c == 0), stop=False)
                        pe.matmul(misc[:, u * 64:u * 64 + XE], k.ones_row[:, :], k.row("ffn_bs"), start=False, stop=True).then_inc(logits, 1)
                        if u == 0:
                            pe.wait_ge(coef_ready, t + 1)
                    pe.wait_ge(coef_ready, 2 * i + 2)
                    for u in range(2):
                        last = pe.transpose(misc[0:XE, 128 + u * P:128 + (u + 1) * P], lg[:, u, 3, :], k.ident[:, :])
                    last.then_inc(coef_turned, 1)
                    pe.wait_ge(coT_ready, i + 1)
                    for e in range(XE + 1):
                        n0 = i * (2 * XE + 2) + 2 * e
                        if e < XE:
                            pe.wait_ge(h_ready, i * XE + e - 1 if e else i * XE)
                            for f in range(FC):
                                for c in range(C):
                                    last = pe.matmul(h_ps[e % 2][:, f * W:(f + 1) * W], w1s[:, c, e * FF + f * P:e * FF + (f + 1) * P],
                                                     xtT[:, c, :], start=(c == 0), stop=(c == C - 1))
                            last.then_inc(h_sum, 1)
                        for u in range(2):
                            b = y_ps[(2 * e + u) % 4]
                            pe.wait_ge(y_read, n0 + u - 3 if 2 * e + u >= 3 else i * (2 * XE + 2))
                            if e == 0:
                                pe.matmul(b[:, :], coT[:, u * P:(u + 1) * P], b2s[:, :], start=True, stop=True).then_inc(y_sum, 1)
                            else:
                                if u == 0:
                                    pe.wait_ge(h_ready, i * XE + e)
                                for f in range(FC):
                                    last = pe.matmul(b[:, :], hT[(e - 1) % 2][:, f, u * P:(u + 1) * P], w2s[:, (e - 1) * FC + f, :],
                                                     start=(f == 0), stop=(f == FC - 1))
                                last.then_inc(y_sum, 1)
        m.end_phase()


def gps_layer(nc, a, out):
    graph_d = nc.dram_tensor("graph_d", [NT, P, NP], F16, kind="Internal").ap()
    res_d = nc.dram_tensor("res_d", [NP, D], F32, kind="Internal").ap()
    mix_d = nc.dram_tensor("mix_d", [NP, D], F32, kind="Internal").ap()
    with ExitStack() as top:
        k = Kept(Memory(nc, top, "kept"))
        build_graph(nc, k, a["src"], a["dst"], a["mask_idx"], a["token"], a["cols"], a["rows"], graph_d)
        big = Memory(nc, top, "s0").sb("big", [P, NT * D])
        x2 = big[:, :].rearrange("p (t n) -> p t n", n=D)
        uT = big[:, :].rearrange("p (c n) -> p c n", n=NP)
        with ExitStack() as s1:
            H = Memory(nc, s1, "s1").sb("H", [P, NT, 2, D], F16)
            HQ = H[:, :, 0, 0:3 * HID].bitcast(BF16).rearrange("p t (h n) -> p t h n", h=3)
            with ExitStack() as s2:
                kvs = Memory(nc, s2, "s2").sb("kvs", [P, D + C])
                norm_and_qkv(nc, k, a["x"], a["token"], a["wqkvT"], H, uT, kvs, res_d)
                attention_out(nc, k, a["woT"], uT, kvs, res_d, mix_d)
            first_convolution(nc, k, graph_d, H, a["w1"], uT)
            batch_norm_relu(nc, k, uT, "g1", "beta1", "bn1")
            with ExitStack() as s2:
                zT = Memory(nc, s2, "s4").sb("zT", [P, 1, NP])
                narrow_features(nc, k, uT, C, a["w2"], HQ, None, "feat2")
                narrow_propagation(nc, k, graph_d, HQ, zT, "b2", "conv2")
                narrow_features(nc, k, zT, 1, a["weT"], HQ, k.kept, "feat3")
                narrow_propagation(nc, k, graph_d, HQ, zT, None, "conv3")
                widen(nc, k, zT, a["w3"], uT)
            batch_norm_relu(nc, k, uT, "g2", "beta2", "bn2")
            last_features(nc, k, uT, a["w4"], H)
            last_convolution(nc, k, graph_d, H, mix_d, x2)
        experts(nc, k, x2, a["ffn_ws"], a["ffn_w1"], a["ffn_w2"], a["ffn_b2"], out)


def lay_out(**a):
    import numpy as np
    f = np.float32
    n = {k.replace("L0_", ""): np.asarray(v) for k, v in a.items()}

    def by_partition(v):
        return v.reshape(-1, P).T

    parts = {"mix_gamma": n["mix_ln_gamma"], "mix_beta": n["mix_ln_beta"], "b1": n["gnn_b1"],
             "g1": n["gnn_g1"], "beta1": n["gnn_beta1"], "b2": n["gnn_b2"], "b3": n["gnn_b3"],
             "g2": n["gnn_g2"], "beta2": n["gnn_beta2"], "ffn_b1": n["ffn_b1"].reshape(-1)}
    rows = {"qkv_b": n["mix_qkv_b"], "out_b": n["mix_out_b"], "b4": n["gnn_b4"], "ffn_bs": n["ffn_bs"]}
    x = np.zeros((NP, D), f)
    x[:N] = n["x"]
    return {
        "x": x, "src": n["src"], "dst": n["dst"],
        "mask_idx": np.ascontiguousarray(n["gnn_mask_idx"].reshape(MP, MC)),
        "token": np.ascontiguousarray(np.broadcast_to(n["gnn_enc_mask_token"], (P, D))),
        "cols": np.ascontiguousarray(np.concatenate([by_partition(parts[c]) for c in COLS], axis=1)),
        "rows": np.concatenate([rows[r] for r in ROWS]).reshape(1, -1),
        "wqkvT": np.ascontiguousarray(n["mix_qkv_w"].T), "woT": np.ascontiguousarray(n["mix_out_w"].T),
        "w1": n["gnn_W1"], "w2": n["gnn_W2"], "weT": np.ascontiguousarray(n["gnn_W_e2d"].T),
        "w3": n["gnn_W3"], "w4": n["gnn_W4"],
        "ffn_ws": n["ffn_Ws"],
        "ffn_w1": np.ascontiguousarray(n["ffn_W1"].transpose(1, 0, 2).reshape(D, XE * FF)),
        "ffn_w2": n["ffn_W2"].reshape(XE * FF, D), "ffn_b2": n["ffn_b2"],
    }


def kernel(**inputs):
    import concourse.bacc as _bacc
    from concourse import mybir as _mybir
    from concourse.bass_utils import run_bass_kernel_spmd as _run

    nc = _bacc.Bacc("TRN2", target_bir_lowering=False, num_devices=1)
    arrays = lay_out(**inputs)
    aps = {name: nc.dram_tensor(name, v.shape, _mybir.dt.from_np(v.dtype), kind="ExternalInput").ap()
           for name, v in arrays.items()}
    out = nc.dram_tensor("out", (NP, D), F32, kind="ExternalOutput").ap()
    gps_layer(nc, aps, out)
    r = _run(nc, [arrays], core_ids=[0])
    return r.results[0]["out"][:N]
```
